# Optimizing a Trainium2 kernel written in Bass

```python
import numpy as np
import jax
import jax.numpy as jnp

def _softmax(x, axis=-1):
    return jax.nn.softmax(x, axis=axis)

def _gelu(x):
    return jax.nn.gelu(x, approximate=True)

def _silu(x):
    return jax.nn.silu(x)

def _sigmoid(x):
    return jax.nn.sigmoid(x)

def _layernorm(x, axis=-1, eps=1e-05):
    m = jnp.mean(x, axis=axis, keepdims=True)
    v = jnp.var(x, axis=axis, keepdims=True)
    return (x - m) / jnp.sqrt(v + eps)

def _scatter_add(tgt, idx, src, axis=0):
    return tgt.at[idx].add(src)

def _segment_sum(src, seg, n):
    return jax.ops.segment_sum(src, seg, n)
kernel_name = 'mk_dlrm_tower_d1_rec_r8_db1482'

def setup_inputs(seed: int=0):
    np.random.seed(seed)
    _w = jnp.asarray

    def _rec_inputs():
        import jax
        import jax.numpy as jnp
        _tk = jax.random.key(seed)
        ids = jnp.stack([jax.random.randint(jax.random.fold_in(_tk, 200 + f), (512,), 0, v, jnp.int32) for f, v in enumerate([1250, 125000, 12500, 1000, 1250, 1250, 1250, 1250, 1000, 12500, 1250, 1250, 12500, 1250, 1000, 12500, 1000, 1250, 12500, 1000, 12500, 12500, 1000, 1000, 1000, 1000])], axis=1)
        tbl_0 = 0.05 * jax.random.normal(jax.random.fold_in(_tk, 500 + 0), (1250, 128), jnp.float32)
        tbl_1 = 0.05 * jax.random.normal(jax.random.fold_in(_tk, 500 + 1), (125000, 128), jnp.float32)
        tbl_2 = 0.05 * jax.random.normal(jax.random.fold_in(_tk, 500 + 2), (12500, 128), jnp.float32)
        tbl_3 = 0.05 * jax.random.normal(jax.random.fold_in(_tk, 500 + 3), (1000, 128), jnp.float32)
        tbl_4 = 0.05 * jax.random.normal(jax.random.fold_in(_tk, 500 + 4), (1250, 128), jnp.float32)
        tbl_5 = 0.05 * jax.random.normal(jax.random.fold_in(_tk, 500 + 5), (1250, 128), jnp.float32)
        tbl_6 = 0.05 * jax.random.normal(jax.random.fold_in(_tk, 500 + 6), (1250, 128), jnp.float32)
        tbl_7 = 0.05 * jax.random.normal(jax.random.fold_in(_tk, 500 + 7), (1250, 128), jnp.float32)
        tbl_8 = 0.05 * jax.random.normal(jax.random.fold_in(_tk, 500 + 8), (1000, 128), jnp.float32)
        tbl_9 = 0.05 * jax.random.normal(jax.random.fold_in(_tk, 500 + 9), (12500, 128), jnp.float32)
        tbl_10 = 0.05 * jax.random.normal(jax.random.fold_in(_tk, 500 + 10), (1250, 128), jnp.float32)
        tbl_11 = 0.05 * jax.random.normal(jax.random.fold_in(_tk, 500 + 11), (1250, 128), jnp.float32)
        tbl_12 = 0.05 * jax.random.normal(jax.random.fold_in(_tk, 500 + 12), (12500, 128), jnp.float32)
        tbl_13 = 0.05 * jax.random.normal(jax.random.fold_in(_tk, 500 + 13), (1250, 128), jnp.float32)
        tbl_14 = 0.05 * jax.random.normal(jax.random.fold_in(_tk, 500 + 14), (1000, 128), jnp.float32)
        tbl_15 = 0.05 * jax.random.normal(jax.random.fold_in(_tk, 500 + 15), (12500, 128), jnp.float32)
        tbl_16 = 0.05 * jax.random.normal(jax.random.fold_in(_tk, 500 + 16), (1000, 128), jnp.float32)
        tbl_17 = 0.05 * jax.random.normal(jax.random.fold_in(_tk, 500 + 17), (1250, 128), jnp.float32)
        tbl_18 = 0.05 * jax.random.normal(jax.random.fold_in(_tk, 500 + 18), (12500, 128), jnp.float32)
        tbl_19 = 0.05 * jax.random.normal(jax.random.fold_in(_tk, 500 + 19), (1000, 128), jnp.float32)
        tbl_20 = 0.05 * jax.random.normal(jax.random.fold_in(_tk, 500 + 20), (12500, 128), jnp.float32)
        tbl_21 = 0.05 * jax.random.normal(jax.random.fold_in(_tk, 500 + 21), (12500, 128), jnp.float32)
        tbl_22 = 0.05 * jax.random.normal(jax.random.fold_in(_tk, 500 + 22), (1000, 128), jnp.float32)
        tbl_23 = 0.05 * jax.random.normal(jax.random.fold_in(_tk, 500 + 23), (1000, 128), jnp.float32)
        tbl_24 = 0.05 * jax.random.normal(jax.random.fold_in(_tk, 500 + 24), (1000, 128), jnp.float32)
        tbl_25 = 0.05 * jax.random.normal(jax.random.fold_in(_tk, 500 + 25), (1000, 128), jnp.float32)
        _rk = jax.random.fold_in(_tk, 7)
        r_dense_features = -0.000292821 + 1.00034 * jax.random.normal(jax.random.fold_in(_rk, 101), (512, 128), jnp.float32)
        W_top1 = 0.0405887 * jax.random.normal(jax.random.fold_in(_tk, 801), (607, 512), jnp.float32)
        W_top2 = 0.0441942 * jax.random.normal(jax.random.fold_in(_tk, 802), (512, 256), jnp.float32)
        W_top3 = 0.0625 * jax.random.normal(jax.random.fold_in(_tk, 803), (256, 1), jnp.float32)
        b_top1 = jnp.zeros((512,), jnp.float32)
        b_top2 = jnp.zeros((256,), jnp.float32)
        return (r_dense_features, ids, tbl_0, tbl_1, tbl_2, tbl_3, tbl_4, tbl_5, tbl_6, tbl_7, tbl_8, tbl_9, tbl_10, tbl_11, tbl_12, tbl_13, tbl_14, tbl_15, tbl_16, tbl_17, tbl_18, tbl_19, tbl_20, tbl_21, tbl_22, tbl_23, tbl_24, tbl_25, W_top1, b_top1, W_top2, b_top2, W_top3)
    r_dense_features, ids, tbl_0, tbl_1, tbl_2, tbl_3, tbl_4, tbl_5, tbl_6, tbl_7, tbl_8, tbl_9, tbl_10, tbl_11, tbl_12, tbl_13, tbl_14, tbl_15, tbl_16, tbl_17, tbl_18, tbl_19, tbl_20, tbl_21, tbl_22, tbl_23, tbl_24, tbl_25, W_top1, b_top1, W_top2, b_top2, W_top3 = _rec_inputs()

    def _L0_rec_setup():
        import jax, jax.numpy as jnp
        import numpy as np
        F = 26
        _TRIU_I, _TRIU_J = np.triu_indices(F + 1, k=1)
        key = jax.random.key(seed)
        k1, k2 = jax.random.split(key)
        B, D = (4096, 128)
        dense_features = jax.random.normal(k1, (B, D), dtype=jnp.float32)
        sparse_features = jax.random.normal(k2, (B, F, D), dtype=jnp.float32)
        return {'dense_features': dense_features, 'sparse_features': sparse_features}
    _L0_rec_all = _L0_rec_setup()
    _L0_rec_in = {k: v for k, v in _L0_rec_all.items() if k in ()}
    del _L0_rec_all
    return {'r_dense_features': r_dense_features, 'ids': ids, 'tbl_0': tbl_0, 'tbl_1': tbl_1, 'tbl_2': tbl_2, 'tbl_3': tbl_3, 'tbl_4': tbl_4, 'tbl_5': tbl_5, 'tbl_6': tbl_6, 'tbl_7': tbl_7, 'tbl_8': tbl_8, 'tbl_9': tbl_9, 'tbl_10': tbl_10, 'tbl_11': tbl_11, 'tbl_12': tbl_12, 'tbl_13': tbl_13, 'tbl_14': tbl_14, 'tbl_15': tbl_15, 'tbl_16': tbl_16, 'tbl_17': tbl_17, 'tbl_18': tbl_18, 'tbl_19': tbl_19, 'tbl_20': tbl_20, 'tbl_21': tbl_21, 'tbl_22': tbl_22, 'tbl_23': tbl_23, 'tbl_24': tbl_24, 'tbl_25': tbl_25, 'W_top1': W_top1, 'b_top1': b_top1, 'W_top2': W_top2, 'b_top2': b_top2, 'W_top3': W_top3}

def reference(r_dense_features, ids, tbl_0, tbl_1, tbl_2, tbl_3, tbl_4, tbl_5, tbl_6, tbl_7, tbl_8, tbl_9, tbl_10, tbl_11, tbl_12, tbl_13, tbl_14, tbl_15, tbl_16, tbl_17, tbl_18, tbl_19, tbl_20, tbl_21, tbl_22, tbl_23, tbl_24, tbl_25, W_top1, b_top1, W_top2, b_top2, W_top3):
    import jax
    import jax.numpy as jnp

    def _L0_rec_ref(dense_features, sparse_features):
        import jax, jax.numpy as jnp
        import numpy as np
        F = 26
        _TRIU_I, _TRIU_J = np.triu_indices(F + 1, k=1)
        combined = jnp.concatenate([dense_features[:, None, :], sparse_features], axis=1)
        interactions = jnp.einsum('bfd,bgd->bfg', combined, combined)
        interactions_flat = interactions[:, _TRIU_I, _TRIU_J]
        return jnp.concatenate([dense_features, interactions_flat], axis=1)
    e = jnp.stack([tbl_0[ids[:, 0]], tbl_1[ids[:, 1]], tbl_2[ids[:, 2]], tbl_3[ids[:, 3]], tbl_4[ids[:, 4]], tbl_5[ids[:, 5]], tbl_6[ids[:, 6]], tbl_7[ids[:, 7]], tbl_8[ids[:, 8]], tbl_9[ids[:, 9]], tbl_10[ids[:, 10]], tbl_11[ids[:, 11]], tbl_12[ids[:, 12]], tbl_13[ids[:, 13]], tbl_14[ids[:, 14]], tbl_15[ids[:, 15]], tbl_16[ids[:, 16]], tbl_17[ids[:, 17]], tbl_18[ids[:, 18]], tbl_19[ids[:, 19]], tbl_20[ids[:, 20]], tbl_21[ids[:, 21]], tbl_22[ids[:, 22]], tbl_23[ids[:, 23]], tbl_24[ids[:, 24]], tbl_25[ids[:, 25]]], axis=1)
    z = _L0_rec_ref(r_dense_features, e)
    z = z.reshape(z.shape[0], -1)
    h = jnp.concatenate([z, r_dense_features], axis=1)
    h = jnp.maximum(h @ W_top1 + b_top1, 0.0)
    h = jnp.maximum(h @ W_top2 + b_top2, 0.0)
    y = h @ W_top3
    return y

_drawn_inputs = setup_inputs


def setup_inputs(seed=0):
    import zlib

    import numpy as np

    out = dict(_drawn_inputs(seed))
    spreads = {'b_top1': (0.0, 0.1), 'b_top2': (0.0, 0.1)}
    factors = {}
    for name, (base, spread) in spreads.items():
        noise = np.random.default_rng([zlib.crc32(name.encode()), seed]).standard_normal(out[name].shape)
        drawn = base * np.exp(spread * noise) if base else spread * noise
        out[name] = jnp.asarray(drawn.astype(out[name].dtype))
    for name, factor in factors.items():
        out[name] = (out[name] * factor).astype(out[name].dtype)
    return out
```

```python
import concourse.bass as bass
from concourse import mybir
from contextlib import ExitStack

B, D = 512, 128
NTBL = 26
F = NTBL + 1
P = 128
NT = B // P
HID1, HID2 = 512, 256
NPAIR = F * (F - 1) // 2
NDIFF = (F - 1) // 2
FW = F + NDIFF
FROWS = 9
KT = F // FROWS
PK = FROWS * NDIFF
QUAD = 32
NQ = P // QUAD
HALF = QUAD // 2
GRP = 4
GROUPS = [(a, min(GRP, NTBL - a)) for a in range(0, NTBL, GRP)]
NG = len(GROUPS)


def pair_rows():
    rows = []
    for f in range(F):
        for d in range(1, NDIFF + 1):
            g = (f + d) % F
            lo, hi = min(f, g), max(f, g)
            rows.append(lo * F - lo * (lo + 1) // 2 + hi - lo - 1)
    return rows


def dlrm_tower(nc, ids, dense, tables, w1pairs, w1dense, b1, w2, b2, w3, out):
    fp32 = mybir.dt.float32
    i32 = mybir.dt.int32
    ALU = mybir.AluOpType
    ACT = mybir.ActivationFunctionType

    ctx = ExitStack()
    with ctx:
        def sb(name, shape, dt=fp32):
            return ctx.enter_context(nc.sbuf_tensor(name, shape, dt))

        def bank(name):
            return ctx.enter_context(nc.psum_tensor(name, [P, 512], fp32))

        def sem(name):
            return ctx.enter_context(nc.semaphore(name))

        gram_dram = nc.dram_tensor("gram_dram", [NT, F, FW, P], fp32, kind="Internal").ap()

        ids_sb = sb("ids_sb", [P, NT, NTBL], i32)
        dense_sb = sb("dense_sb", [P, NT, D])
        rows = sb("rows", [P, NT, NTBL, D])
        XT = sb("XT", [P, NT, P * F + QUAD - F])
        denseT = sb("denseT", [P, NT, P])
        gram = sb("gram", [P, 2, FW, QUAD])
        Z = sb("Z", [PK, NT, KT, P])
        w1p = sb("w1p", [PK, KT, HID1])
        w1d = sb("w1d", [P, 2, HID1])
        w1s = sb("w1s", [P, HID1])
        w2_sb = sb("w2_sb", [P, HID1 // P, HID2])
        w3_sb = sb("w3_sb", [P, HID2 // P])
        b1_sb = sb("b1_sb", [P, HID1 // P])
        b2_sb = sb("b2_sb", [P, HID2 // P])
        h1 = sb("h1", [P, 2, HID1 // P, P])
        h2 = sb("h2", [P, 2, HID2 // P, P])
        y_sb = sb("y_sb", [1, B])
        ident = sb("ident", [P, P])

        tp_bank = [bank("tp0"), bank("tp1")]
        gram_bank = [bank("gram0"), bank("gram1")]
        h1_bank = [bank("h1a"), bank("h1b")]
        h2_bank = bank("h2b")

        ids_in = sem("ids_in")
        dense_in = sem("dense_in")
        w1_in = sem("w1_in")
        w_in = sem("w_in")
        rows_in = [[sem(f"rows_in{t}_{j}") for j in range(NG)] for t in range(NT)]
        id_zero = sem("id_zero")
        ident_ready = sem("ident_ready")
        pad_ready = sem("pad_ready")
        w1s_ready = sem("w1s_ready")
        transposed = sem("transposed")
        xt_dve = sem("xt_dve")
        xt_act = sem("xt_act")
        gram_done = sem("gram_done")
        gram_dve = sem("gram_dve")
        gram_act = sem("gram_act")
        gram_out = [sem(f"gram_out{t}") for t in range(NT)]
        z_in = [sem(f"z_in{t}") for t in range(NT)]
        h1_done = sem("h1_done")
        h1_act = sem("h1_act")
        h1_dve = sem("h1_dve")
        h2_done = sem("h2_done")
        h2_act = sem("h2_act")
        y_done = sem("y_done")
        y_dve = sem("y_dve")
        out_done = sem("out_done")

        def fill(t, j):
            return 1 + t * NG + j

        def dve_fills(n):
            return (n + 1) // 2

        def act_fills(n):
            return n // 2

        def xt_view(t):
            return XT[:, t, 0:P * F].rearrange("d (s f) -> d f s", f=F)

        block = ctx.enter_context(nc.Block())

        @block.sync
        def _(sp):
            sp.dma_start(ids_sb[:, :, :], ids.rearrange("(t p) f -> p t f", p=P)).then_inc(ids_in, 16)
            sp.dma_start(dense_sb[:, :, :], dense.rearrange("(t p) d -> p t d", p=P)).then_inc(dense_in, 16)
            sp.dma_start(w1d[:, :, :], w1dense.rearrange("(a p) n -> p a n", p=P)).then_inc(w1_in, 16)
            sp.dma_start(w1p[:, :, :], w1pairs.rearrange("(k p) n -> p k n", p=PK)).then_inc(w_in, 16)
            sp.dma_start(w2_sb[:, :, :], w2.rearrange("(c p) n -> p c n", p=P)).then_inc(w_in, 16)
            sp.dma_start(b1_sb[:, :], b1).then_inc(w_in, 16)
            sp.dma_start(b2_sb[:, :], b2).then_inc(w_in, 16)
            sp.dma_start(w3_sb[:, :], w3).then_inc(w_in, 16)
            for t in range(NT):
                sp.wait_ge(gram_dve, t + 1)
                sp.wait_ge(gram_act, t + 1)
                for q in range(NQ):
                    sp.dma_start(gram_dram[t, :, :, q * QUAD:(q + 1) * QUAD],
                                 gram[q * QUAD:q * QUAD + F, t % 2, :, :]).then_inc(gram_out[t], 16)
                sp.wait_ge(gram_out[t], 16 * NQ)
                for k in range(KT):
                    f0 = k * FROWS
                    src = bass.AP(gram_dram.tensor, ((t * F + f0) * FW + f0 + 1) * P,
                                  [[(FW + 1) * P, FROWS], [P, NDIFF], [1, P]])
                    sp.dma_start(Z[:, t, k, :], src).then_inc(z_in[t], 16)
            sp.wait_ge(y_dve, NT)
            sp.dma_start(out, y_sb[:, :]).then_inc(out_done, 16)
            sp.wait_ge(out_done, 16)

        @block.gpsimd
        def _(pool):
            nc.gpsimd.memset(ident[:, :], 0.0).then_inc(id_zero, 1)
            pool.wait_ge(id_zero, 1)
            nc.gpsimd.affine_select(out=ident[:, :], in_=ident[:, :], compare_op=ALU.not_equal, fill=1.0,
                                    base=0, pattern=[[-1, P]], channel_multiplier=1).then_inc(ident_ready, 1)
            pool.wait_ge(ids_in, 16)
            for t in range(NT):
                for j, (a, n) in enumerate(GROUPS):
                    for f in range(a, a + n):
                        pool.indirect_dma_start(
                            rows[:, t, f, :], None, tables[f],
                            bass.IndirectOffsetOnAxis(ap=ids_sb[:, t, f:f + 1], axis=0)).then_inc(rows_in[t][j], 16)

        @block.tensor
        def _(pe):
            def transposes(t, j):
                n = fill(t, j)
                a, cnt = GROUPS[j]
                pe.wait_ge(rows_in[t][j], 16 * cnt)
                if n % 2 == 0:
                    pe.wait_ge(xt_dve, dve_fills(n))
                elif n > 1:
                    pe.wait_ge(xt_act, act_fills(n))
                for c in range(cnt):
                    last = nc.tensor.transpose(tp_bank[n % 2][:, c * P:(c + 1) * P], rows[:, t, a + c, :], ident[:, :])
                last.then_inc(transposed, 1)

            def grams(t):
                n = fill(t, NG)
                pe.wait_ge(xt_dve, dve_fills(n))
                pe.wait_ge(xt_act, act_fills(n))
                for h in range(2):
                    if t >= 1:
                        pe.wait_ge(gram_dve if h == 0 else gram_act, t)
                    for s in range(HALF):
                        for q in range(NQ):
                            p = QUAD * q + HALF * h + s
                            last = nc.tensor.matmul(
                                gram_bank[h][QUAD * q:QUAD * (q + 1), s * F:(s + 1) * F],
                                XT[:, t, p * F:p * F + QUAD], XT[:, t, p * F:(p + 1) * F], start=True, stop=True)
                    last.then_inc(gram_done, 1)

            def mlp(t):
                pe.wait_ge(z_in[t], 16 * KT)
                for m in range(HID1 // P):
                    if m % 2 == 0 and t >= 1:
                        pe.wait_ge(h1_act if m == 0 else h1_dve, t)
                    ps = h1_bank[m // 2][:, (m % 2) * P:(m % 2 + 1) * P]
                    nc.tensor.matmul(ps, w1s[:, m * P:(m + 1) * P], denseT[:, t, :], start=True, stop=False)
                    for k in range(KT):
                        last = nc.tensor.matmul(ps, w1p[:, k, m * P:(m + 1) * P], Z[:, t, k, :],
                                                start=False, stop=(k == KT - 1))
                    if m % 2:
                        last.then_inc(h1_done, 1)
                pe.wait_ge(h1_act, t + 1)
                pe.wait_ge(h1_dve, t + 1)
                if t >= 1:
                    pe.wait_ge(y_dve, t)
                for m in range(HID2 // P):
                    for k in range(HID1 // P):
                        last = nc.tensor.matmul(h2_bank[:, m * P:(m + 1) * P], w2_sb[:, k, m * P:(m + 1) * P],
                                                h1[:, t % 2, k, :], start=(k == 0), stop=(k == HID1 // P - 1))
                last.then_inc(h2_done, 1)
                pe.wait_ge(h2_act, t + 1)
                for k in range(HID2 // P):
                    last = nc.tensor.matmul(h2_bank[0:1, HID2:HID2 + P], w3_sb[:, k:k + 1], h2[:, t % 2, k, :],
                                            start=(k == 0), stop=(k == HID2 // P - 1))
                last.then_inc(y_done, 1)

            pe.wait_ge(ident_ready, 1)
            pe.wait_ge(dense_in, 16)
            for t in range(NT):
                last = nc.tensor.transpose(tp_bank[0][:, t * P:(t + 1) * P], dense_sb[:, t, :], ident[:, :])
            last.then_inc(transposed, 1)
            pe.wait_ge(pad_ready, 1)
            pe.wait_ge(w1s_ready, 1)
            pe.wait_ge(w_in, 16 * 5)
            for t in range(NT):
                for j in range(NG):
                    transposes(t, j)
                    if j == 2 and t >= 1:
                        mlp(t - 1)
                grams(t)
            mlp(NT - 1)

        @block.vector
        def _(dve):
            def empty_fill(t, j):
                n = fill(t, j)
                a, cnt = GROUPS[j]
                dve.wait_ge(transposed, n + 1)
                nc.vector.tensor_copy(xt_view(t)[:, 1 + a:1 + a + cnt, :],
                                      tp_bank[0][:, 0:cnt * P].rearrange("d (f s) -> d f s", f=cnt)).then_inc(xt_dve, 1)

            nc.vector.memset(XT[:, :, P * F:], 0.0).then_inc(pad_ready, 1)
            dve.wait_ge(transposed, 1)
            nc.vector.tensor_copy(XT[:, :, 0:P * F].rearrange("d t (s f) -> d t s f", f=F)[:, :, :, 0],
                                  tp_bank[0][:, :].rearrange("d (t s) -> d t s", t=NT))
            nc.vector.tensor_copy(denseT[:, :, :], tp_bank[0][:, :].rearrange("d (t s) -> d t s", t=NT)).then_inc(xt_dve, 1)
            dve.wait_ge(w1_in, 16)
            nc.vector.tensor_add(w1s[:, :], w1d[:, 0, :], w1d[:, 1, :]).then_inc(w1s_ready, 1)

            def h1_relu(t):
                dve.wait_ge(h1_done, 2 * t + 2)
                for m in (2, 3):
                    last = nc.vector.tensor_scalar(h1[:, t % 2, m, :], h1_bank[1][:, (m - 2) * P:(m - 1) * P],
                                                   b1_sb[:, m:m + 1], 0.0, ALU.add, ALU.max)
                last.then_inc(h1_dve, 1)

            def y_copy(t):
                dve.wait_ge(y_done, t + 1)
                nc.vector.tensor_copy(y_sb[0:1, t * P:(t + 1) * P], h2_bank[0:1, HID2:HID2 + P]).then_inc(y_dve, 1)

            dve.wait_ge(w_in, 16 * 5)
            for t in range(NT):
                for j in range(NG):
                    if fill(t, j) % 2 == 0:
                        empty_fill(t, j)
                    if j == 2 and t >= 1:
                        h1_relu(t - 1)
                        y_copy(t - 1)
                dve.wait_ge(gram_done, 2 * t + 1)
                if t >= 2:
                    dve.wait_ge(gram_out[t - 2], 16 * NQ)
                g = gram_bank[0][:, 0:HALF * F].rearrange("p (s g) -> p g s", g=F)
                nc.vector.tensor_copy(gram[:, t % 2, 0:F, 0:HALF], g)
                nc.vector.tensor_copy(gram[:, t % 2, F:FW, 0:HALF], g[:, 0:NDIFF, :]).then_inc(gram_dve, 1)
            h1_relu(NT - 1)
            y_copy(NT - 1)

        @block.scalar
        def _(act):
            def empty_fill(t, j):
                n = fill(t, j)
                a, cnt = GROUPS[j]
                act.wait_ge(transposed, n + 1)
                nc.scalar.copy(xt_view(t)[:, 1 + a:1 + a + cnt, :],
                               tp_bank[1][:, 0:cnt * P].rearrange("d (f s) -> d f s", f=cnt)).then_inc(xt_act, 1)

            def relus(t):
                act.wait_ge(h1_done, 2 * t + 1)
                for m in (0, 1):
                    last = nc.scalar.activation(h1[:, t % 2, m, :], h1_bank[0][:, m * P:(m + 1) * P], ACT.Relu,
                                                bias=b1_sb[:, m:m + 1])
                last.then_inc(h1_act, 1)
                act.wait_ge(h2_done, t + 1)
                for m in range(HID2 // P):
                    last = nc.scalar.activation(h2[:, t % 2, m, :], h2_bank[:, m * P:(m + 1) * P], ACT.Relu,
                                                bias=b2_sb[:, m:m + 1])
                last.then_inc(h2_act, 1)

            act.wait_ge(w_in, 16 * 5)
            for t in range(NT):
                for j in range(NG):
                    if fill(t, j) % 2:
                        empty_fill(t, j)
                    if j == 2 and t >= 1:
                        relus(t - 1)
                act.wait_ge(gram_done, 2 * t + 2)
                if t >= 2:
                    act.wait_ge(gram_out[t - 2], 16 * NQ)
                g = gram_bank[1][:, 0:HALF * F].rearrange("p (s g) -> p g s", g=F)
                nc.scalar.copy(gram[:, t % 2, 0:F, HALF:], g)
                nc.scalar.copy(gram[:, t % 2, F:FW, HALF:], g[:, 0:NDIFF, :]).then_inc(gram_act, 1)
            relus(NT - 1)


def kernel(**inputs):
    import numpy as np
    import concourse.bacc as bacc
    from concourse import mybir as mb
    from concourse.bass_utils import run_bass_kernel_spmd

    nc = bacc.Bacc("TRN2", target_bir_lowering=False, num_devices=1)
    w1 = np.asarray(inputs["W_top1"])
    laid = {
        "ids": np.asarray(inputs["ids"]),
        "dense": np.asarray(inputs["r_dense_features"]),
        "w1pairs": w1[D:D + NPAIR][pair_rows()],
        "w1dense": np.concatenate([w1[0:D], w1[D + NPAIR:]], axis=0),
        "b1": np.asarray(inputs["b_top1"]).reshape(HID1 // P, P).T,
        "w2": np.asarray(inputs["W_top2"]),
        "b2": np.asarray(inputs["b_top2"]).reshape(HID2 // P, P).T,
        "w3": np.asarray(inputs["W_top3"]).reshape(HID2 // P, P).T,
    }
    for f in range(NTBL):
        laid[f"tbl_{f}"] = np.asarray(inputs[f"tbl_{f}"])
    arrays, aps = {}, {}
    for name, a in laid.items():
        a = np.ascontiguousarray(a)
        arrays[f"in_{name}"] = a
        aps[name] = nc.dram_tensor(f"in_{name}", a.shape, mb.dt.from_np(a.dtype), kind="ExternalInput").ap()
    out = nc.dram_tensor("out_0", (1, B), mb.dt.float32, kind="ExternalOutput").ap()
    dlrm_tower(nc, aps["ids"], aps["dense"], [aps[f"tbl_{f}"] for f in range(NTBL)], aps["w1pairs"],
               aps["w1dense"], aps["b1"], aps["w2"], aps["b2"], aps["w3"], out)
    r = run_bass_kernel_spmd(nc, [arrays], core_ids=[0])
    return r.results[0]["out_0"].reshape(B, 1)
```

```python
import concourse.bass as bass
from concourse import mybir
from contextlib import ExitStack

B, D = 512, 128
ROWS = [1250, 125000, 12500, 1000, 1250, 1250, 1250, 1250, 1000, 12500, 1250, 1250, 12500, 1250, 1000, 12500,
        1000, 1250, 12500, 1000, 12500, 12500, 1000, 1000, 1000, 1000]
NTBL = len(ROWS)
F = NTBL + 1
P = 128
NT = B // P
HOT = [f for f in range(NTBL) if ROWS[f] == min(ROWS)]
COLD = [f for f in range(NTBL) if f not in HOT]
ORDER = HOT + COLD
NH, NC = len(HOT), len(COLD)
HROWS = min(ROWS)
HJ = 8
HP = HROWS // HJ
ACT_J = [6, 7]
DVE_J = [j for j in range(HJ) if j not in ACT_J]
PE_J = [0, 1, 6, 2, 3, 7, 4, 5]
HID1, HID2 = 512, 256
M1, M2 = HID1 // P, HID2 // P
NPAIR = F * (F - 1) // 2
NDIFF = (F - 1) // 2
FW = F + NDIFF
FROWS = 9
KT = F // FROWS
PK = FROWS * NDIFF
QUAD = 32
NQ = P // QUAD
SPB = 8
NB = QUAD // SPB
GRP = 4
GROUPS = [(a, min(GRP, NC - a)) for a in range(0, NC, GRP)]
NG = len(GROUPS)
FILLS = [(t, j) for t in range(NT) for j in range(NG)]
W_LOADS = 5


def due(o):
    return max(0, (7 * o) // 5)


def pair_rows():
    place = [0] + [1 + t for t in ORDER]
    rows = []
    for f in range(F):
        for d in range(1, NDIFF + 1):
            a, b = place[f], place[(f + d) % F]
            lo, hi = min(a, b), max(a, b)
            rows.append(lo * F - lo * (lo + 1) // 2 + hi - lo - 1)
    return rows


def dlrm_tower(nc, ids, dense, tables, w1pairs, w1dense, b1, w2, b2, w3, out):
    fp32 = mybir.dt.float32
    fp32r = mybir.dt.float32r
    i32 = mybir.dt.int32
    ALU = mybir.AluOpType
    ACT = mybir.ActivationFunctionType

    ctx = ExitStack()
    with ctx:
        def sb(name, shape, dt=fp32):
            return ctx.enter_context(nc.sbuf_tensor(name, shape, dt))

        def bank(name):
            return ctx.enter_context(nc.psum_tensor(name, [P, 512], fp32))

        def sem(name):
            return ctx.enter_context(nc.semaphore(name))

        gram_dram = nc.dram_tensor("gram_dram", [NT, F, FW, P], fp32, kind="Internal").ap()

        ids_sb = sb("ids_sb", [P, NT, NTBL], i32)
        ids_f = sb("ids_f", [P, NT, NH])
        idsT = sb("idsT", [NH, B], fp32r)
        dense_sb = sb("dense_sb", [P, NT, D])
        rows = sb("rows", [P, NT, NC, D])
        XT = sb("XT", [P, NT, P, QUAD])
        denseT = sb("denseT", [P, NT, P])
        table = sb("table", [HP, 2, HJ, D])
        high = sb("high", [HP, 2, HJ, D], fp32r)
        low = sb("low", [HP, 2, HJ, D], fp32r)
        onehot = sb("onehot", [HP, HJ, B], fp32r)
        dist = sb("dist", [HP, 2, B])
        row_id = sb("row_id", [HP, HJ])
        row_id_i = sb("row_id_i", [HP, HJ], i32)
        minus_row_id = sb("minus_row_id", [HP, HJ])
        gram = sb("gram", [P, 2, 2, FW, QUAD])
        Z = sb("Z", [PK, NT, KT, P])
        w1p = sb("w1p", [PK, KT, HID1])
        w1d = sb("w1d", [P, 2, HID1])
        w1s = sb("w1s", [P, HID1])
        w2_sb = sb("w2_sb", [P, M1, HID2])
        w3_sb = sb("w3_sb", [P, M2])
        b1_sb = sb("b1_sb", [P, M1])
        b2_sb = sb("b2_sb", [P, M2])
        h1 = sb("h1", [P, M1, P])
        h2 = sb("h2", [P, M2, P])
        y_sb = sb("y_sb", [1, B])
        ident = sb("ident", [P, P])
        ident_r = sb("ident_r", [NH, NH], fp32r)

        tp_bank = [bank("tp0"), bank("tp1")]
        gram_bank = [bank("gram0"), bank("gram1")]
        h1_bank = [bank("h1a"), bank("h1b")]
        h2_bank = bank("h2b")
        look_bank = gram_bank
        bcast_bank = h1_bank
        idsT_bank = h2_bank
        bcast_act_bank = bank("bcast_act")

        ids_in = sem("ids_in")
        dense_in = sem("dense_in")
        table_in = [sem("table_in0"), sem("table_in1")]
        w1_in = sem("w1_in")
        w_in = sem("w_in")
        rows_in = [[sem(f"rows_in{t}_{j}") for j in range(NG)] for t in range(NT)]
        id_zero = sem("id_zero")
        ident_ready = sem("ident_ready")
        iota_ready = sem("iota_ready")
        row_id_ready = sem("row_id_ready")
        ids_f_ready = sem("ids_f_ready")
        idsT_ready = sem("idsT_ready")
        idsT_used = sem("idsT_used")
        pad_ready = sem("pad_ready")
        w1s_ready = sem("w1s_ready")
        high_ready = sem("high_ready")
        low_ready = sem("low_ready")
        bcast_ready = sem("bcast_ready")
        bcast_act_ready = sem("bcast_act_ready")
        dist_ready = sem("dist_ready")
        hot_dve = sem("hot_dve")
        hot_act = sem("hot_act")
        hot_used = sem("hot_used")
        look_out = sem("look_out")
        transposed = sem("transposed")
        xt_in = sem("xt_in")
        gram_done = sem("gram_done")
        gram_in = sem("gram_in")
        gram_out = [sem(f"gram_out{t}") for t in range(NT)]
        z_in = [sem(f"z_in{t}") for t in range(NT)]
        h1_done = sem("h1_done")
        h1_act = sem("h1_act")
        h1_dve = sem("h1_dve")
        h2_done = sem("h2_done")
        h2_act = sem("h2_act")
        y_done = sem("y_done")
        y_dve = sem("y_dve")
        out_done = sem("out_done")

        def slots(t):
            return XT[:, t, :, :].rearrange("d (r a) f -> d f a r", a=2)

        block = ctx.enter_context(nc.Block())

        @block.sync
        def _(sp):
            def load_table(o):
                if o >= 2:
                    sp.wait_ge(low_ready, o - 1)
                sp.dma_start(table[:, o % 2, :, :],
                             tables[HOT[o]].rearrange("(p j) d -> p j d", j=HJ)).then_inc(table_in[o % 2], 16)

            sp.dma_start(ids_sb[:, :, :], ids.rearrange("(t p) f -> p t f", p=P)).then_inc(ids_in, 16)
            load_table(0)
            sp.dma_start(dense_sb[:, :, :], dense.rearrange("(t p) d -> p t d", p=P)).then_inc(dense_in, 16)
            load_table(1)
            sp.dma_start(w1d[:, :, :], w1dense.rearrange("(a p) n -> p a n", p=P)).then_inc(w1_in, 16)
            sp.dma_start(w1p[:, :, :], w1pairs.rearrange("(k p) n -> p k n", p=PK)).then_inc(w_in, 16)
            sp.dma_start(w2_sb[:, :, :], w2.rearrange("(c p) n -> p c n", p=P)).then_inc(w_in, 16)
            sp.dma_start(b1_sb[:, :], b1).then_inc(w_in, 16)
            sp.dma_start(b2_sb[:, :], b2).then_inc(w_in, 16)
            sp.dma_start(w3_sb[:, :], w3).then_inc(w_in, 16)
            for o in range(2, NH):
                load_table(o)
            for t in range(NT):
                sp.wait_ge(gram_in, NB * (t + 1))
                for q in range(NQ):
                    c = 64 * (q % 2) + QUAD * (q // 2)
                    sp.dma_start(gram_dram[t, :, :, c:c + QUAD],
                                 gram[q * QUAD:q * QUAD + F, t % 2, q % 2, :, :]).then_inc(gram_out[t], 16)
                sp.wait_ge(gram_out[t], 16 * NQ)
                for k in range(KT):
                    f0 = k * FROWS
                    src = bass.AP(gram_dram.tensor, ((t * F + f0) * FW + f0 + 1) * P,
                                  [[(FW + 1) * P, FROWS], [P, NDIFF], [1, P]])
                    sp.dma_start(Z[:, t, k, :], src).then_inc(z_in[t], 16)
            sp.wait_ge(y_dve, NT)
            sp.dma_start(out, y_sb[:, :]).then_inc(out_done, 16)
            sp.wait_ge(out_done, 16)

        @block.gpsimd
        def _(pool):
            nc.gpsimd.memset(ident[:, :], 0.0).then_inc(id_zero, 1)
            nc.gpsimd.iota(row_id_i[:, :], pattern=[[1, HJ]], base=0, channel_multiplier=HJ).then_inc(iota_ready, 1)
            pool.wait_ge(id_zero, 1)
            nc.gpsimd.affine_select(out=ident[:, :], in_=ident[:, :], compare_op=ALU.not_equal, fill=1.0,
                                    base=0, pattern=[[-1, P]], channel_multiplier=1).then_inc(ident_ready, 1)
            pool.wait_ge(ids_in, 16)
            for t in range(NT):
                for j, (a, n) in enumerate(GROUPS):
                    for c in range(a, a + n):
                        pool.indirect_dma_start(
                            rows[:, t, c, :], None, tables[COLD[c]],
                            bass.IndirectOffsetOnAxis(ap=ids_sb[:, t, NH + c:NH + c + 1], axis=0)
                        ).then_inc(rows_in[t][j], 16)

        @block.tensor
        def _(pe):
            def transposes(n):
                t, j = FILLS[n - 1]
                a, cnt = GROUPS[j]
                pe.wait_ge(rows_in[t][j], 16 * cnt)
                if n >= 2:
                    pe.wait_ge(xt_in, n - 1)
                for c in range(cnt):
                    last = nc.tensor.transpose(tp_bank[n % 2][:, c * P:(c + 1) * P], rows[:, t, a + c, :], ident[:, :])
                last.then_inc(transposed, 1)

            def broadcast_ids(o):
                select = ident_r[:, o:o + 1].to_broadcast([NH, HP])
                if o >= 1:
                    pe.wait_ge(dist_ready, len(ACT_J) * o)
                nc.tensor.matmul(bcast_act_bank[0:HP, :], select, idsT[:, :], start=True,
                                 stop=True).then_inc(bcast_act_ready, 1)
                if o >= 2:
                    pe.wait_ge(hot_dve, len(DVE_J) * (o - 1))
                nc.tensor.matmul(bcast_bank[o % 2][0:HP, :], select, idsT[:, :], start=True,
                                 stop=True).then_inc(bcast_ready, 1)

            def lookup(o):
                pe.wait_ge(low_ready, o + 1)
                if o >= 2:
                    pe.wait_ge(look_out, o - 1)
                for i, j in enumerate(PE_J):
                    if j in ACT_J:
                        pe.wait_ge(hot_act, len(ACT_J) * o + ACT_J.index(j) + 1)
                    else:
                        pe.wait_ge(hot_dve, len(DVE_J) * o + DVE_J.index(j) + 1)
                    nc.tensor.matmul(look_bank[o % 2][:, :], high[:, o % 2, j, :], onehot[:, j, :],
                                     start=(i == 0), stop=False)
                    last = nc.tensor.matmul(look_bank[o % 2][:, :], low[:, o % 2, j, :], onehot[:, j, :],
                                            start=False, stop=(i == HJ - 1))
                    last.then_inc(hot_used, 1)

            def grams(t):
                pe.wait_ge(xt_in, 1 + (t + 1) * NG)
                pe.wait_ge(look_out, NH)
                for i in range(NB):
                    n = NB * t + i
                    if n >= 2:
                        pe.wait_ge(gram_in, n - 1)
                    for s in range(SPB):
                        for b in range(2):
                            slot = 2 * (QUAD * b + SPB * i + s)
                            last = nc.tensor.matmul(
                                gram_bank[n % 2][64 * b:64 * (b + 1), s * 2 * F:(s + 1) * 2 * F],
                                XT[:, t, slot:slot + 2, :].rearrange("d a f -> d (a f)"),
                                XT[:, t, slot:slot + 2, 0:F], start=True, stop=True)
                    last.then_inc(gram_done, 1)

            def mlp(t):
                pe.wait_ge(z_in[t], 16 * KT)
                for m in range(M1):
                    if m % 2 == 0 and t >= 1:
                        pe.wait_ge(h1_act if m == 0 else h1_dve, t)
                    ps = h1_bank[m // 2][:, (m % 2) * P:(m % 2 + 1) * P]
                    nc.tensor.matmul(ps, w1s[:, m * P:(m + 1) * P], denseT[:, t, :], start=True, stop=False)
                    for k in range(KT):
                        last = nc.tensor.matmul(ps, w1p[:, k, m * P:(m + 1) * P], Z[:, t, k, :],
                                                start=False, stop=(k == KT - 1))
                    if m % 2:
                        last.then_inc(h1_done, 1)
                pe.wait_ge(h1_act, t + 1)
                pe.wait_ge(h1_dve, t + 1)
                if t >= 1:
                    pe.wait_ge(y_dve, t)
                for m in range(M2):
                    for k in range(M1):
                        last = nc.tensor.matmul(h2_bank[:, m * P:(m + 1) * P], w2_sb[:, k, m * P:(m + 1) * P],
                                                h1[:, k, :], start=(k == 0), stop=(k == M1 - 1))
                last.then_inc(h2_done, 1)
                pe.wait_ge(h2_act, t + 1)
                for k in range(M2):
                    last = nc.tensor.matmul(h2_bank[0:1, HID2:HID2 + P], w3_sb[:, k:k + 1], h2[:, k, :],
                                            start=(k == 0), stop=(k == M2 - 1))
                last.then_inc(y_done, 1)

            pe.wait_ge(ident_ready, 1)
            pe.wait_ge(ids_f_ready, 1)
            for t in range(NT):
                last = nc.tensor.transpose(idsT_bank[0:NH, t * P:(t + 1) * P], ids_f[:, t, :], ident[:, :])
            last.then_inc(idsT_ready, 1)
            pe.wait_ge(idsT_used, 1)
            broadcast_ids(0)
            pe.wait_ge(dense_in, 16)
            for t in range(NT):
                last = nc.tensor.transpose(tp_bank[0][:, t * P:(t + 1) * P], dense_sb[:, t, :], ident[:, :])
            last.then_inc(transposed, 1)
            for o in range(NH):
                if o + 1 < NH:
                    broadcast_ids(o + 1)
                lookup(o)
                for n in range(due(o - 1), due(o)):
                    transposes(1 + n)
            pe.wait_ge(pad_ready, 1)
            pe.wait_ge(w1s_ready, 1)
            pe.wait_ge(w_in, 16 * W_LOADS)
            grams(0)
            grams(1)
            for n in range(due(NH - 1), 3 * NG):
                transposes(1 + n)
            grams(2)
            mlp(0)
            transposes(1 + 3 * NG)
            transposes(2 + 3 * NG)
            mlp(1)
            for n in range(3 * NG + 2, 4 * NG):
                transposes(1 + n)
            grams(3)
            mlp(2)
            mlp(3)

        @block.vector
        def _(dve):
            def lower_part(o):
                dve.wait_ge(high_ready, o + 1)
                nc.vector.tensor_tensor(low[:, o % 2, :, :], table[:, o % 2, :, :],
                                        high[:, o % 2, :, :].bitcast(fp32), ALU.subtract).then_inc(low_ready, 1)

            def compare(o):
                dve.wait_ge(bcast_ready, o + 1)
                for j in DVE_J:
                    if o >= 1:
                        dve.wait_ge(hot_used, HJ * (o - 1) + PE_J.index(j) + 1)
                    nc.vector.tensor_scalar(onehot[:, j, :], bcast_bank[o % 2][0:HP, :], row_id[:, j:j + 1], None,
                                            ALU.is_equal).then_inc(hot_dve, 1)

            def empty_grams(t):
                if t >= 2:
                    dve.wait_ge(gram_out[t - 2], 16 * NQ)
                for i in range(NB):
                    n = NB * t + i
                    dve.wait_ge(gram_done, n + 1)
                    for a in range(2):
                        g = gram_bank[n % 2][:, 0:SPB * 2 * F].rearrange("p (s a g) -> p a g s", a=2, g=F)[:, a]
                        dst = gram[:, t % 2, a, :, i * SPB:(i + 1) * SPB]
                        nc.vector.tensor_copy(dst[:, 0:F, :], g)
                        last = nc.vector.tensor_copy(dst[:, F:FW, :], g[:, 0:NDIFF, :])
                    last.then_inc(gram_in, 1)

            def relu_half(t):
                dve.wait_ge(h1_done, 2 * t + 2)
                for m in (2, 3):
                    last = nc.vector.tensor_scalar(h1[:, m, :], h1_bank[1][:, (m - 2) * P:(m - 1) * P],
                                                   b1_sb[:, m:m + 1], 0.0, ALU.add, ALU.max)
                last.then_inc(h1_dve, 1)

            def y_copy(t):
                dve.wait_ge(y_done, t + 1)
                nc.vector.tensor_copy(y_sb[0:1, t * P:(t + 1) * P], h2_bank[0:1, HID2:HID2 + P]).then_inc(y_dve, 1)

            dve.wait_ge(iota_ready, 1)
            nc.vector.tensor_copy(row_id[:, :], row_id_i[:, :]).then_inc(row_id_ready, 1)
            dve.wait_ge(row_id_ready, 1)
            nc.vector.tensor_scalar(minus_row_id[:, :], row_id[:, :], -1.0, None, ALU.mult).then_inc(row_id_ready, 1)
            dve.wait_ge(ident_ready, 1)
            nc.vector.tensor_copy(ident_r[:, :], ident[0:NH, 0:NH])
            dve.wait_ge(ids_in, 16)
            nc.vector.tensor_copy(ids_f[:, :, :], ids_sb[:, :, 0:NH]).then_inc(ids_f_ready, 1)
            dve.wait_ge(idsT_ready, 1)
            nc.vector.tensor_copy(idsT[:, :], idsT_bank[0:NH, :]).then_inc(idsT_used, 1)
            nc.vector.memset(XT[:, :, :, F:].rearrange("d t p f -> d (t p) f"), 0.0).then_inc(pad_ready, 1)
            lower_part(0)
            for o in range(NH):
                compare(o)
                if o + 1 < NH:
                    lower_part(o + 1)
            dve.wait_ge(w1_in, 16)
            nc.vector.tensor_add(w1s[:, :], w1d[:, 0, :], w1d[:, 1, :]).then_inc(w1s_ready, 1)
            dve.wait_ge(w_in, 16 * W_LOADS)
            empty_grams(0)
            empty_grams(1)
            empty_grams(2)
            relu_half(0)
            y_copy(0)
            relu_half(1)
            y_copy(1)
            empty_grams(3)
            relu_half(2)
            y_copy(2)
            relu_half(3)
            y_copy(3)

        @block.scalar
        def _(act):
            def empty_fill(n):
                t, j = FILLS[n - 1]
                a, cnt = GROUPS[j]
                act.wait_ge(transposed, n + 1)
                f = 1 + NH + a
                nc.scalar.copy(slots(t)[:, f:f + cnt],
                               tp_bank[n % 2][:, 0:cnt * P].rearrange("d (f a r) -> d f a r", f=cnt, a=2)).then_inc(xt_in, 1)

            def higher_part(o):
                act.wait_ge(table_in[o % 2], 16 * (o // 2 + 1))
                if o >= 2:
                    act.wait_ge(hot_used, HJ * (o - 1))
                nc.scalar.copy(high[:, o % 2, :, :], table[:, o % 2, :, :]).then_inc(high_ready, 1)

            def compare(o):
                act.wait_ge(bcast_act_ready, o + 1)
                for i, j in enumerate(ACT_J):
                    if o >= 1:
                        act.wait_ge(hot_act, len(ACT_J) * (o - 1) + i + 1)
                    nc.scalar.activation(dist[:, i, :], bcast_act_bank[0:HP, :], ACT.Abs,
                                         bias=minus_row_id[:, j:j + 1]).then_inc(dist_ready, 1)
                for i, j in enumerate(ACT_J):
                    n = len(ACT_J) * o + i
                    act.wait_ge(dist_ready, n + 1)
                    if o >= 1:
                        act.wait_ge(hot_used, HJ * (o - 1) + PE_J.index(j) + 1)
                    nc.scalar.activation(onehot[:, j, :], dist[:, i, :], ACT.Relu, bias=1.0,
                                         scale=-1.0).then_inc(hot_act, 1)

            def empty_lookup(o):
                act.wait_ge(hot_used, HJ * (o + 1))
                nc.scalar.copy(XT[:, :, :, 1 + o].rearrange("d t (r a) -> d t a r", a=2),
                               look_bank[o % 2][:, :].rearrange("d (t a r) -> d t a r", t=NT, a=2)).then_inc(look_out, 1)

            def relus(t):
                act.wait_ge(h1_done, 2 * t + 1)
                for m in (0, 1):
                    last = nc.scalar.activation(h1[:, m, :], h1_bank[0][:, m * P:(m + 1) * P], ACT.Relu,
                                                bias=b1_sb[:, m:m + 1])
                last.then_inc(h1_act, 1)
                act.wait_ge(h2_done, t + 1)
                for m in range(M2):
                    last = nc.scalar.activation(h2[:, m, :], h2_bank[:, m * P:(m + 1) * P], ACT.Relu,
                                                bias=b2_sb[:, m:m + 1])
                last.then_inc(h2_act, 1)

            higher_part(0)
            act.wait_ge(row_id_ready, 2)
            for o in range(NH):
                compare(o)
                if o == 0:
                    act.wait_ge(transposed, 1)
                    src = tp_bank[0][:, :].rearrange("d (t a r) -> d t a r", t=NT, a=2)
                    nc.scalar.copy(XT[:, :, :, 0].rearrange("d t (r a) -> d t a r", a=2), src)
                    nc.scalar.copy(denseT[:, :, :], tp_bank[0][:, :].rearrange("d (t s) -> d t s", t=NT)).then_inc(xt_in, 1)
                if o + 1 < NH:
                    higher_part(o + 1)
                if o >= 1:
                    empty_lookup(o - 1)
                    for n in range(due(o - 2), due(o - 1)):
                        empty_fill(1 + n)
            empty_lookup(NH - 1)
            for n in range(due(NH - 2), 3 * NG):
                empty_fill(1 + n)
            act.wait_ge(w_in, 16 * W_LOADS)
            relus(0)
            empty_fill(1 + 3 * NG)
            empty_fill(2 + 3 * NG)
            relus(1)
            for n in range(3 * NG + 2, 4 * NG):
                empty_fill(1 + n)
            relus(2)
            relus(3)


def kernel(**inputs):
    import numpy as np
    import concourse.bacc as bacc
    from concourse import mybir as mb
    from concourse.bass_utils import run_bass_kernel_spmd

    nc = bacc.Bacc("TRN2", target_bir_lowering=False, num_devices=1)
    w1 = np.asarray(inputs["W_top1"])
    laid = {
        "ids": np.asarray(inputs["ids"])[:, ORDER],
        "dense": np.asarray(inputs["r_dense_features"]),
        "w1pairs": w1[D:D + NPAIR][pair_rows()],
        "w1dense": np.concatenate([w1[0:D], w1[D + NPAIR:]], axis=0),
        "b1": np.asarray(inputs["b_top1"]).reshape(M1, P).T,
        "w2": np.asarray(inputs["W_top2"]),
        "b2": np.asarray(inputs["b_top2"]).reshape(M2, P).T,
        "w3": np.asarray(inputs["W_top3"]).reshape(M2, P).T,
    }
    for f in range(NTBL):
        laid[f"tbl_{f}"] = np.asarray(inputs[f"tbl_{f}"])
    arrays, aps = {}, {}
    for name, a in laid.items():
        a = np.ascontiguousarray(a)
        arrays[f"in_{name}"] = a
        aps[name] = nc.dram_tensor(f"in_{name}", a.shape, mb.dt.from_np(a.dtype), kind="ExternalInput").ap()
    out = nc.dram_tensor("out_0", (1, B), mb.dt.float32, kind="ExternalOutput").ap()
    dlrm_tower(nc, aps["ids"], aps["dense"], [aps[f"tbl_{f}"] for f in range(NTBL)], aps["w1pairs"],
               aps["w1dense"], aps["b1"], aps["w2"], aps["b2"], aps["w3"], out)
    r = run_bass_kernel_spmd(nc, [arrays], core_ids=[0])
    return r.results[0]["out_0"].reshape(B, 1)
```

```python
import concourse.bass as bass
from concourse import mybir
from contextlib import ExitStack

B, D = 512, 128
ROWS = [1250, 125000, 12500, 1000, 1250, 1250, 1250, 1250, 1000, 12500, 1250, 1250, 12500, 1250, 1000, 12500,
        1000, 1250, 12500, 1000, 12500, 12500, 1000, 1000, 1000, 1000]
NTBL = len(ROWS)
F = NTBL + 1
P = 128
NT = B // P
HOT = [f for f in range(NTBL) if ROWS[f] == min(ROWS)]
COLD = [f for f in range(NTBL) if f not in HOT]
ORDER = HOT + COLD
NH, NC = len(HOT), len(COLD)
HROWS = min(ROWS)
HJ = 8
HP = HROWS // HJ
PE_J = [0, 1, 6, 2, 5, 7, 3, 4]
ACT_J = [[5, 6, 7] if o in (1, 3, 5, 7) else [6, 7] for o in range(NH)]
DVE_J = [[j for j in PE_J if j not in ACT_J[o]] for o in range(NH)]
MAX_ACT_J = max(len(js) for js in ACT_J)
HID1, HID2 = 512, 256
M1 = HID1 // P
NPAIR = F * (F - 1) // 2
NDIFF = (F - 1) // 2
FROWS = 9
KT = F // FROWS
PK = FROWS * NDIFF
QUAD = 32
NQ = P // QUAD
SPB = 8
NB = QUAD // SPB
GRP = P // QUAD
NQTR = P // QUAD
QG = (NC - 1) // GRP
assert (NC - 1) % GRP == 0 and QUAD // NQTR == SPB
FILLS_T = 1 + NQTR
FILLS = [(t, [0] if j == 0 else list(range(1 + QG * (j - 1), 1 + QG * j))) for t in range(NT) for j in range(FILLS_T)]
FILLS = FILLS[:-1] + [(NT - 1, list(range(NC - QG, NC - 1))), (NT - 1, [NC - 1])]
NFILL = len(FILLS)
NGRAM = NT * NB + 1
BASE = [sum(ROWS[COLD[i]] for i in range(c)) for c in range(NC)]
MID = 5
DENSE_AFTER = [1, 2, 5, NH - 1]
IDS_RING = 3
W_LOADS = 5
WARM_UP = 16
assert KT == 3
LAST_LAYER1 = [(0, m) for m in range(M1)] + [(1, 0), (1, 1), (2, 0), (2, 1)]
LAST_LAYER1 += [(k, m) for m in range(2, M1) for k in (1, 2)]


def gram_steps(t, i):
    if t < NT - 1 or i < NB - 1:
        return range(SPB * i, SPB * (i + 1))
    first = SPB * (NB - 1) + (i - NB + 1) * SPB // 2
    return range(first, first + SPB // 2)


def made(tiles, o):
    return sum(len(js) for js in tiles[:o + 1])


def pair_rows():
    place = [0] + [1 + t for t in ORDER]
    rows = []
    flat = [f * F + f + d for f in range(F - 1) for d in range(1, NDIFF + 1)]
    flat += [f * F + f + NDIFF + 1 for f in range(NDIFF)]
    for x in flat:
        a, b = place[x // F], place[x % F]
        lo, hi = min(a, b), max(a, b)
        rows.append(lo * F - lo * (lo + 1) // 2 + hi - lo - 1)
    assert sorted(rows) == list(range(NPAIR))
    return rows


def dlrm_tower(nc, ids_cold, ids_hot, dense, cold_table, hot_tables, w1pairs, w1dense, b1, w2, b2, w3, out):
    fp32 = mybir.dt.float32
    fp32r = mybir.dt.float32r
    i32 = mybir.dt.int32
    ALU = mybir.AluOpType
    ACT = mybir.ActivationFunctionType

    ctx = ExitStack()
    with ctx:
        def sb(name, shape, dt=fp32):
            return ctx.enter_context(nc.sbuf_tensor(name, shape, dt))

        def bank(name):
            return ctx.enter_context(nc.psum_tensor(name, [P, 512], fp32))

        def sem(name):
            return ctx.enter_context(nc.semaphore(name))

        gram_dram = nc.dram_tensor("gram_dram", [NT, F, F, P], fp32, kind="Internal").ap()

        ids_sb = sb("ids_sb", [P, 2, NT, NC], i32)
        cold_row = sb("cold_row", [P, NT, NC], i32)
        ids_all = sb("ids_all", [HP, IDS_RING, B], i32)
        rows = sb("rows", [P, NT, NC, D])
        XT = sb("XT", [P, NT, P, QUAD])
        denseT = sb("denseT", [P, NT, P])
        table = sb("table", [HP, 2, HJ, D])
        high = sb("high", [HP, 2, HJ, D], fp32r)
        low = sb("low", [HP, 2, HJ, D], fp32r)
        onehot = sb("onehot", [HP, HJ, B], fp32r)
        dist = sb("dist", [HP, MAX_ACT_J, B])
        row_id_i = sb("row_id_i", [HP, HJ], i32)
        minus_row_id = sb("minus_row_id", [HP, HJ])
        gram = sb("gram", [P, 2, 2, F, QUAD])
        Z = sb("Z", [PK, NT, KT, P])
        w1p = sb("w1p", [PK, KT, HID1])
        w1d = sb("w1d", [P, 2, HID1])
        from_dense = sb("from_dense", [P, M1, B])
        w1s = sb("w1s", [P, HID1])
        w2_sb = sb("w2_sb", [P, M1, HID2])
        w3_sb = sb("w3_sb", [P, HID2])
        b1_sb = sb("b1_sb", [P, M1])
        b2_sb = sb("b2_sb", [P, HID2])
        h1 = sb("h1", [P, 2, M1, P])
        h2 = sb("h2", [P, HID2])
        h2_w3 = sb("h2_w3", [P, HID2])
        y_sb = sb("y_sb", [P, NT])
        ident = sb("ident", [P, P])

        tp_bank = bank("tp")
        aux_bank = bank("aux")
        gram_bank = [bank("gram0"), bank("gram1")]
        h1_bank = [bank(f"h1_{m}") for m in range(M1)]
        h1_ps = [b[:, 0:P] for b in h1_bank]
        look_bank = gram_bank
        row_id_ps = aux_bank[0:HP, 0:HJ]
        h2_ps = aux_bank[:, 0:HID2]

        def tp_ps(n):
            return tp_bank if n < NFILL - 1 else gram_bank[(NGRAM - 2) % 2]

        ids_in = sem("ids_in")
        ids_all_in = [sem(f"ids_all_in{i}") for i in range(IDS_RING)]
        dense_in = sem("dense_in")
        table_in = [sem("table_in0"), sem("table_in1")]
        w1_in = sem("w1_in")
        w_in = sem("w_in")
        rows_in = [sem(f"rows_in{n}") for n in range(NFILL)]
        cold_row_ready = sem("cold_row_ready")
        id_zero = sem("id_zero")
        ident_ready = sem("ident_ready")
        iota_ready = sem("iota_ready")
        row_id_ready = sem("row_id_ready")
        minus_ready = sem("minus_ready")
        pad_ready = sem("pad_ready")
        w1s_ready = sem("w1s_ready")
        high_ready = sem("high_ready")
        low_ready = sem("low_ready")
        dist_ready = sem("dist_ready")
        hot_dve = sem("hot_dve")
        hot_act = sem("hot_act")
        hot_used = sem("hot_used")
        look_out = sem("look_out")
        transposed = sem("transposed")
        dense_xt = sem("dense_xt")
        xt_in = sem("xt_in")
        gram_done = sem("gram_done")
        gram_in = sem("gram_in")
        gram_out = [sem(f"gram_out{t}") for t in range(NT)]
        gram_out_pool = sem("gram_out_pool")
        z_in = [sem(f"z_in{t}") for t in range(NT - 1)]
        z_in_last = [sem(f"z_in_last{k}") for k in range(KT)]
        diagonal_in_last = sem("diagonal_in_last")
        dense_done = sem("dense_done")
        dense_in_sb = sem("dense_in_sb")
        dense_added = sem("dense_added")
        h1_done = sem("h1_done")
        h1_in = sem("h1_in")
        h2_done = sem("h2_done")
        h2_in = sem("h2_in")
        y_in = sem("y_in")
        out_done = sem("out_done")

        def slots(t):
            return XT[:, t, :, :].rearrange("d (r a) f -> d f a r", a=2)

        def quarter(t, gathers):
            i, k = (gathers[0] - 1) // QG, (gathers[0] - 1) % QG
            f = 2 + NH + k * GRP
            w = 2 * SPB
            return XT[:, t, :, f:f + GRP * len(gathers)].rearrange("d (b i r) f -> d f b i r", b=2, r=w)[:, :, :, i]

        def write_products(eng, t, q, written):
            c = 64 * (q % 2) + QUAD * (q // 2)
            eng.dma_start(gram_dram[t, :, :, c:c + QUAD],
                          gram[q * QUAD:q * QUAD + F, t % 2, q % 2, :, :]).then_inc(written, 16)

        def read_back(eng, t, k):
            f0 = k * FROWS
            n = min(FROWS, F - 1 - f0)
            src = bass.AP(gram_dram.tensor, ((t * F + f0) * F + f0 + 1) * P,
                          [[(F + 1) * P, n], [P, NDIFF], [1, P]])
            eng.dma_start(Z[0:n * NDIFF, t, k, :], src).then_inc(z_in[t] if t < NT - 1 else z_in_last[k], 16)

        def read_diagonal(eng, t):
            src = bass.AP(gram_dram.tensor, (t * F * F + NDIFF + 1) * P, [[(F + 1) * P, NDIFF], [1, P]])
            eng.dma_start(Z[PK - NDIFF:, t, KT - 1, :], src).then_inc(z_in[t] if t < NT - 1 else diagonal_in_last, 16)

        block = ctx.enter_context(nc.Block())

        @block.sync
        def _(sp):
            def load_table(o):
                if o >= 2:
                    sp.wait_ge(low_ready, o - 1)
                sp.dma_start(table[:, o % 2, :, :],
                             hot_tables[o].rearrange("(p j) d -> p j d", j=HJ)).then_inc(table_in[o % 2], 16)

            def load_ids(o):
                if o >= IDS_RING:
                    sp.wait_ge(hot_dve, made(DVE_J, o - IDS_RING))
                    sp.wait_ge(dist_ready, made(ACT_J, o - IDS_RING))
                sp.dma_start(ids_all[:, o % IDS_RING, :],
                             ids_hot[o, :].partition_broadcast(HP)).then_inc(ids_all_in[o % IDS_RING], 16)

            sp.dma_start(ids_sb[:, :, :, :], ids_cold).then_inc(ids_in, 16)
            load_table(0)
            load_ids(1)
            load_table(1)
            sp.dma_start(denseT[:, :, :], dense.rearrange("d (t p) -> d t p", p=P)).then_inc(dense_in, 16)
            sp.dma_start(w1d[:, :, :], w1dense.rearrange("(a p) n -> p a n", p=P)).then_inc(w1_in, 16)
            load_ids(2)
            load_table(2)
            load_ids(3)
            load_table(3)
            load_ids(4)
            sp.dma_start(w1p[:, :, :], w1pairs.rearrange("(k p) n -> p k n", p=PK)).then_inc(w_in, 16)
            load_table(4)
            load_ids(5)
            sp.dma_start(w2_sb[:, :, :], w2.rearrange("(c p) n -> p c n", p=P)).then_inc(w_in, 16)
            sp.dma_start(b1_sb[:, :], b1).then_inc(w_in, 16)
            sp.dma_start(b2_sb[:, :], b2.partition_broadcast(P)).then_inc(w_in, 16)
            sp.dma_start(w3_sb[:, :], w3.partition_broadcast(P)).then_inc(w_in, 16)
            for o in range(5, NH):
                load_table(o)
                if o + 1 < NH:
                    load_ids(o + 1)
            for t in range(NT):
                sp.wait_ge(gram_in, NB * (t + 1) if t < NT - 1 else NGRAM)
                for q in range(NQ):
                    if t < NT - 1 or q < NQ - 1:
                        write_products(sp, t, q, gram_out[t])
                if t < NT - 1:
                    sp.wait_ge(gram_out[t], 16 * NQ)
                else:
                    sp.wait_ge(gram_out[t], 16 * (NQ - 1))
                    sp.wait_ge(gram_out_pool, 16)
                for k in range(KT):
                    read_back(sp, t, k)
                if t < NT - 1:
                    read_diagonal(sp, t)
            sp.wait_ge(y_in, NT)
            sp.dma_start(out, y_sb[:, :]).then_inc(out_done, 16)
            sp.wait_ge(out_done, 16)

        @block.gpsimd
        def _(pool):
            nc.gpsimd.memset(ident[:, :], 0.0).then_inc(id_zero, 1)
            nc.gpsimd.iota(row_id_i[:, :], pattern=[[1, HJ]], base=0, channel_multiplier=HJ).then_inc(iota_ready, 1)
            pool.wait_ge(id_zero, 1)
            nc.gpsimd.affine_select(out=ident[:, :], in_=ident[:, :], compare_op=ALU.not_equal, fill=1.0,
                                    base=0, pattern=[[-1, P]], channel_multiplier=1).then_inc(ident_ready, 1)
            pool.wait_ge(cold_row_ready, 1)
            for n, (t, gathers) in enumerate(FILLS):
                for c in gathers:
                    pool.indirect_dma_start(
                        rows[:, t, c, :], None, cold_table,
                        bass.IndirectOffsetOnAxis(ap=cold_row[:, t, c:c + 1], axis=0)
                    ).then_inc(rows_in[n], 16)
            pool.wait_ge(gram_in, NGRAM)
            write_products(pool, NT - 1, NQ - 1, gram_out_pool)
            pool.wait_ge(gram_out[NT - 1], 16 * (NQ - 1))
            pool.wait_ge(gram_out_pool, 16)
            read_diagonal(pool, NT - 1)

        @block.tensor
        def _(pe):
            def transposes(n):
                t, gathers = FILLS[n]
                pe.wait_ge(rows_in[n], 16 * len(gathers))
                if n == NFILL - 1:
                    pe.wait_ge(gram_in, NGRAM - 3)
                elif n >= 1:
                    pe.wait_ge(xt_in, n)
                for i, c in enumerate(gathers):
                    last = nc.tensor.transpose(tp_ps(n)[:, i * P:(i + 1) * P], rows[:, t, c, :], ident[:, :])
                last.then_inc(transposed, 1)

            def lookup(o):
                pe.wait_ge(low_ready, o + 1)
                if o >= 2:
                    pe.wait_ge(look_out, o - 1)
                for i, j in enumerate(PE_J):
                    if j in ACT_J[o]:
                        pe.wait_ge(hot_act, o + 1)
                    else:
                        pe.wait_ge(hot_dve, made(DVE_J, o - 1) + DVE_J[o].index(j) + 1)
                    nc.tensor.matmul(look_bank[o % 2][:, :], high[:, o % 2, j, :], onehot[:, j, :],
                                     start=(i == 0), stop=False)
                    last = nc.tensor.matmul(look_bank[o % 2][:, :], low[:, o % 2, j, :], onehot[:, j, :],
                                            start=False, stop=(i == HJ - 1))
                    last.then_inc(hot_used, 1)
                    if i == MID:
                        transposes(o)

            def dense_layer1(m):
                nc.tensor.matmul(h1_bank[m][:, :], w1s[:, m * P:(m + 1) * P],
                                 denseT[:, :, :].rearrange("d t p -> d (t p)"), start=True, stop=True).then_inc(dense_done, 1)

            def grams(t, i):
                n = NB * t + i
                pe.wait_ge(xt_in, t * FILLS_T + i + 2 if n < NGRAM - 2 else NFILL)
                if n >= 2:
                    pe.wait_ge(gram_in, n - 1)
                for s, step in enumerate(gram_steps(t, i)):
                    for b in range(2):
                        slot = 2 * (QUAD * b + step)
                        last = nc.tensor.matmul(
                            gram_bank[n % 2][64 * b:64 * b + QUAD + F, s * 2 * F:(s + 1) * 2 * F],
                            XT[:, t, slot:slot + 2, :].rearrange("d a f -> d (a f)")[:, 0:QUAD + F],
                            XT[:, t, slot:slot + 2, 0:F], start=True, stop=True)
                last.then_inc(gram_done, 1)

            def layer1(t, m):
                if m == 0:
                    pe.wait_ge(z_in[t], 16 * (KT + 1))
                if t == 0:
                    pe.wait_ge(dense_in_sb, m + 1)
                else:
                    pe.wait_ge(h1_in, M1 * (t - 1) + m + 1)
                for k in range(KT):
                    last = nc.tensor.matmul(h1_ps[m], w1p[:, k, m * P:(m + 1) * P],
                                            Z[:, t, k, :], start=(k == 0), stop=(k == KT - 1))
                last.then_inc(h1_done, 1)

            def layer2(t, k):
                pe.wait_ge(h1_in, M1 * t + k + 1)
                if k == 0 and t >= 1:
                    pe.wait_ge(h2_in, t)
                last = nc.tensor.matmul(h2_ps, h1[:, t % 2, k, :], w2_sb[:, k, :], start=(k == 0), stop=(k == M1 - 1))
                if k == M1 - 1:
                    last.then_inc(h2_done, 1)

            pe.wait_ge(ident_ready, 1)
            for _ in range(WARM_UP):
                nc.tensor.matmul(tp_bank[:, 0:P], ident[:, :], ident[:, :], start=True, stop=True)
            for o in range(NH):
                lookup(o)
                if o == DENSE_AFTER[0]:
                    pe.wait_ge(w1s_ready, 1)
                    pe.wait_ge(dense_in, 16)
                if o in DENSE_AFTER:
                    dense_layer1(DENSE_AFTER.index(o))
            pe.wait_ge(look_out, NH)
            pe.wait_ge(dense_xt, 1)
            pe.wait_ge(pad_ready, NT)
            pe.wait_ge(w_in, 16 * W_LOADS)
            transposes(9)
            grams(0, 0)
            transposes(10)
            grams(0, 1)
            transposes(11)
            grams(0, 2)
            grams(0, 3)
            transposes(12)
            grams(1, 0)
            transposes(13)
            grams(1, 1)
            grams(1, 2)
            grams(1, 3)
            grams(2, 0)
            transposes(14)
            grams(2, 1)
            grams(2, 2)
            transposes(15)
            grams(2, 3)
            layer1(0, 0)
            transposes(16)
            layer1(0, 1)
            layer2(0, 0)
            grams(3, 0)
            layer1(0, 2)
            layer2(0, 1)
            transposes(17)
            layer1(0, 3)
            layer2(0, 2)
            grams(3, 1)
            transposes(18)
            layer1(1, 0)
            grams(3, 2)
            transposes(19)
            layer1(1, 1)
            transposes(20)
            layer2(0, 3)
            grams(3, 3)
            grams(3, 4)
            layer1(1, 2)
            layer1(1, 3)
            layer2(1, 0)
            layer2(1, 1)
            layer2(1, 2)
            layer2(1, 3)
            layer1(2, 0)
            layer1(2, 1)
            layer1(2, 2)
            layer1(2, 3)
            layer2(2, 0)
            layer2(2, 1)
            layer2(2, 2)
            layer2(2, 3)
            for k, m in LAST_LAYER1:
                pe.wait_ge(z_in_last[k], 16)
                if k == 0:
                    pe.wait_ge(h1_in, M1 * (NT - 2) + m + 1)
                if k == KT - 1:
                    pe.wait_ge(diagonal_in_last, 16)
                last = nc.tensor.matmul(h1_ps[m], w1p[:, k, m * P:(m + 1) * P], Z[:, NT - 1, k, :],
                                        start=(k == 0), stop=(k == KT - 1))
                if k == KT - 1:
                    last.then_inc(h1_done, 1)
            for k in range(M1):
                layer2(NT - 1, k)

        @block.vector
        def _(dve):
            def lower_part(o):
                dve.wait_ge(high_ready, o + 1)
                nc.vector.tensor_tensor(low[:, o % 2, :, :], table[:, o % 2, :, :],
                                        high[:, o % 2, :, :].bitcast(fp32), ALU.subtract).then_inc(low_ready, 1)

            def compare(o, tiles):
                if tiles[0] == 0:
                    dve.wait_ge(ids_all_in[o % IDS_RING], 16 * (o // IDS_RING + 1))
                for j in tiles:
                    if o >= 1:
                        dve.wait_ge(hot_used, HJ * (o - 1) + PE_J.index(j) + 1)
                    nc.vector.tensor_tensor(onehot[:, j, :], ids_all[:, o % IDS_RING, :],
                                            row_id_ps[:, j:j + 1].to_broadcast([HP, B]),
                                            ALU.is_equal).then_inc(hot_dve, 1)

            def empty_grams(t, i):
                n = NB * t + i
                if i == 0 and t >= 2:
                    dve.wait_ge(gram_out[t - 2], 16 * NQ)
                dve.wait_ge(gram_done, n + 1)
                steps = gram_steps(t, i)
                for a in range(2):
                    g = gram_bank[n % 2][:, 0:len(steps) * 2 * F].rearrange("p (s a g) -> p a g s", a=2, g=F)[:, a]
                    last = nc.vector.tensor_copy(gram[:, t % 2, a, :, steps[0]:steps[0] + len(steps)], g)
                last.then_inc(gram_in, 1)

            def add_dense(t, m):
                dve.wait_ge(h1_done, M1 * t + m + 1)
                if t == 0:
                    dve.wait_ge(dense_in_sb, m + 1)
                nc.vector.tensor_tensor(h1_ps[m], h1_ps[m], from_dense[:, m, t * P:(t + 1) * P],
                                        ALU.add).then_inc(dense_added, 1)

            def output(t):
                dve.wait_ge(h2_done, t + 1)
                if t >= 1:
                    dve.wait_ge(y_in, t)
                nc.vector.tensor_tensor(h2[:, :], h2_ps, b2_sb[:, :], ALU.add).then_inc(h2_in, 1)
                dve.wait_ge(h2_in, t + 1)
                nc.vector.scalar_tensor_tensor(h2_w3[:, :], h2[:, :], 0.0, w3_sb[:, :], ALU.max, ALU.mult,
                                               accum_out=y_sb[:, t:t + 1]).then_inc(y_in, 1)

            def clear_pad(t):
                nc.vector.memset(XT[:, t, :, F:], 0.0).then_inc(pad_ready, 1)

            clear_pad(0)
            clear_pad(1)
            dve.wait_ge(iota_ready, 1)
            nc.vector.tensor_copy(row_id_ps, row_id_i[:, :]).then_inc(row_id_ready, 1)
            clear_pad(2)
            dve.wait_ge(ids_in, 16)
            nc.vector.tensor_add(cold_row[:, :, :], ids_sb[:, 0, :, :], ids_sb[:, 1, :, :]).then_inc(cold_row_ready, 1)
            clear_pad(3)
            dve.wait_ge(row_id_ready, 1)
            compare(0, DVE_J[0][:HJ // 2])
            lower_part(0)
            compare(0, DVE_J[0][HJ // 2:])
            for o in range(1, NH):
                lower_part(o)
                if o == 1:
                    dve.wait_ge(w1_in, 16)
                    nc.vector.tensor_add(w1s[:, :], w1d[:, 0, :], w1d[:, 1, :]).then_inc(w1s_ready, 1)
                compare(o, DVE_J[o])
            empty_grams(0, 0)
            empty_grams(0, 1)
            empty_grams(0, 2)
            empty_grams(0, 3)
            empty_grams(1, 0)
            empty_grams(1, 1)
            empty_grams(1, 2)
            empty_grams(1, 3)
            empty_grams(2, 0)
            empty_grams(2, 1)
            empty_grams(2, 2)
            empty_grams(2, 3)
            add_dense(0, 0)
            add_dense(0, 1)
            empty_grams(3, 0)
            add_dense(0, 2)
            add_dense(0, 3)
            empty_grams(3, 1)
            add_dense(1, 0)
            empty_grams(3, 2)
            add_dense(1, 1)
            empty_grams(3, 3)
            empty_grams(3, 4)
            output(0)
            add_dense(1, 2)
            add_dense(1, 3)
            output(1)
            add_dense(2, 0)
            add_dense(2, 1)
            add_dense(2, 2)
            add_dense(2, 3)
            output(2)
            for m in range(M1):
                add_dense(3, m)
            output(3)

        @block.scalar
        def _(act):
            def empty_fill(n):
                t, gathers = FILLS[n]
                act.wait_ge(transposed, n + 1)
                x = tp_ps(n)[:, 0:len(gathers) * P]
                if gathers == [0]:
                    nc.scalar.copy(slots(t)[:, 1 + NH], x.rearrange("d (a r) -> d a r", a=2)).then_inc(xt_in, 1)
                else:
                    nc.scalar.copy(quarter(t, gathers),
                                   x.rearrange("d (f b r) -> d f b r", b=2, r=2 * SPB)).then_inc(xt_in, 1)

            def higher_part(o):
                act.wait_ge(table_in[o % 2], 16 * (o // 2 + 1))
                if o >= 2:
                    act.wait_ge(hot_used, HJ * (o - 1))
                nc.scalar.copy(high[:, o % 2, :, :], table[:, o % 2, :, :]).then_inc(high_ready, 1)

            def distances(o):
                act.wait_ge(ids_all_in[o % IDS_RING], 16 * (o // IDS_RING + 1))
                if o >= 1:
                    act.wait_ge(hot_act, o)
                for i, j in enumerate(ACT_J[o]):
                    nc.scalar.activation(dist[:, i, :], ids_all[:, o % IDS_RING, :], ACT.Abs,
                                         bias=minus_row_id[:, j:j + 1]).then_inc(dist_ready, 1)

            def compare(o):
                act.wait_ge(dist_ready, made(ACT_J, o))
                if o >= 1:
                    act.wait_ge(hot_used, HJ * (o - 1) + max(PE_J.index(j) for j in ACT_J[o]) + 1)
                nc.scalar.activation(onehot[:, ACT_J[o][0]:HJ, :], dist[:, 0:len(ACT_J[o]), :], ACT.Relu, bias=1.0,
                                     scale=-1.0).then_inc(hot_act, 1)

            def empty_lookup(o):
                act.wait_ge(hot_used, HJ * (o + 1))
                nc.scalar.copy(XT[:, :, :, 1 + o].rearrange("d t (r a) -> d t a r", a=2),
                               look_bank[o % 2][:, :].rearrange("d (t a r) -> d t a r", t=NT, a=2)).then_inc(look_out, 1)

            def keep_dense(m):
                act.wait_ge(dense_done, m + 1)
                nc.scalar.activation(from_dense[:, m, :], h1_bank[m][:, :], ACT.Identity,
                                     bias=b1_sb[:, m:m + 1]).then_inc(dense_in_sb, 1)

            def relu1(t, m):
                act.wait_ge(dense_added, M1 * t + m + 1)
                nc.scalar.activation(h1[:, t % 2, m, :], h1_ps[m], ACT.Relu).then_inc(h1_in, 1)

            act.dma_start(ids_all[:, 0, :], ids_hot[0, :].partition_broadcast(HP)).then_inc(ids_all_in[0], 16)
            act.wait_ge(iota_ready, 1)
            nc.scalar.activation(minus_row_id[:, :], row_id_i[:, :], ACT.Identity, scale=-1.0).then_inc(minus_ready, 1)
            act.wait_ge(minus_ready, 1)
            distances(0)
            higher_part(0)
            for o in range(NH):
                if o >= 1:
                    distances(o)
                    empty_fill(o - 1)
                compare(o)
                if o + 1 < NH:
                    higher_part(o + 1)
                if o == 0:
                    act.wait_ge(dense_in, 16)
                    nc.scalar.copy(XT[:, :, :, 0].rearrange("d t (r a) -> d t a r", a=2),
                                   denseT[:, :, :].rearrange("d t (a r) -> d t a r", a=2)).then_inc(dense_xt, 1)
                else:
                    empty_lookup(o - 1)
            empty_fill(NH - 1)
            empty_lookup(NH - 1)
            empty_fill(9)
            empty_fill(10)
            empty_fill(11)
            empty_fill(12)
            act.wait_ge(w_in, 16 * W_LOADS)
            keep_dense(0)
            empty_fill(13)
            keep_dense(1)
            empty_fill(14)
            keep_dense(2)
            empty_fill(15)
            keep_dense(3)
            relu1(0, 0)
            empty_fill(16)
            relu1(0, 1)
            relu1(0, 2)
            empty_fill(17)
            relu1(0, 3)
            empty_fill(18)
            relu1(1, 0)
            empty_fill(19)
            empty_fill(20)
            relu1(1, 1)
            relu1(1, 2)
            relu1(1, 3)
            relu1(2, 0)
            relu1(2, 1)
            relu1(2, 2)
            relu1(2, 3)
            for m in range(M1):
                relu1(3, m)


def kernel(**inputs):
    import numpy as np
    import concourse.bacc as bacc
    from concourse import mybir as mb
    from concourse.bass_utils import run_bass_kernel_spmd

    nc = bacc.Bacc("TRN2", target_bir_lowering=False, num_devices=1)
    w1 = np.asarray(inputs["W_top1"])
    ids = np.asarray(inputs["ids"])

    def gather_order(x):
        whole = x[:, 0].reshape(NT, P).transpose(1, 0)[:, :, None]
        v = x[:, 1:].reshape(NT, 2, 2, NQTR, SPB, QG, GRP)
        quarters = v.transpose(6, 2, 4, 1, 0, 3, 5).reshape(P, NT, NQTR * QG)
        return np.concatenate([whole, quarters], axis=2)

    laid = {
        "ids_cold": np.stack([gather_order(ids[:, COLD]),
                              gather_order(np.broadcast_to(np.array(BASE, ids.dtype), (B, NC)))], axis=1),
        "cold_table": np.concatenate([np.asarray(inputs[f"tbl_{f}"]) for f in COLD]),
        "ids_hot": ids[:, HOT].T,
        "dense": np.asarray(inputs["r_dense_features"]).T,
        "w1pairs": w1[D:D + NPAIR][pair_rows()],
        "w1dense": np.concatenate([w1[0:D], w1[D + NPAIR:]], axis=0),
        "b1": np.asarray(inputs["b_top1"]).reshape(M1, P).T,
        "w2": np.asarray(inputs["W_top2"]),
        "b2": np.asarray(inputs["b_top2"]),
        "w3": np.asarray(inputs["W_top3"]).reshape(HID2),
    }
    for f in HOT:
        laid[f"tbl_{f}"] = np.asarray(inputs[f"tbl_{f}"])
    arrays, aps = {}, {}
    for name, a in laid.items():
        a = np.ascontiguousarray(a)
        arrays[f"in_{name}"] = a
        aps[name] = nc.dram_tensor(f"in_{name}", a.shape, mb.dt.from_np(a.dtype), kind="ExternalInput").ap()
    out = nc.dram_tensor("out_0", (P, NT), mb.dt.float32, kind="ExternalOutput").ap()
    dlrm_tower(nc, aps["ids_cold"], aps["ids_hot"], aps["dense"], aps["cold_table"], [aps[f"tbl_{f}"] for f in HOT], aps["w1pairs"],
               aps["w1dense"], aps["b1"], aps["w2"], aps["b2"], aps["w3"], out)
    r = run_bass_kernel_spmd(nc, [arrays], core_ids=[0])
    return r.results[0]["out_0"].T.reshape(B, 1)
```
